# Optimizing a Trainium2 kernel written in Bass

```python
import numpy as np
import jax
import jax.numpy as jnp

def _softmax(x, axis=-1):
    return jax.nn.softmax(x, axis=axis)
def _gelu(x):
    return jax.nn.gelu(x, approximate=True)
def _silu(x):
    return jax.nn.silu(x)
def _sigmoid(x):
    return jax.nn.sigmoid(x)
def _layernorm(x, axis=-1, eps=1e-5):
    m = jnp.mean(x, axis=axis, keepdims=True)
    v = jnp.var(x, axis=axis, keepdims=True)
    return (x - m) / jnp.sqrt(v + eps)
def _scatter_add(tgt, idx, src, axis=0):
    return tgt.at[idx].add(src)
def _segment_sum(src, seg, n):
    return jax.ops.segment_sum(src, seg, n)

kernel_name = 'mk_conv_preact_d2_conv_nchw32_80de15'

def setup_inputs(seed: int = 0):
    np.random.seed(seed)
    _w = jnp.asarray
    def _rec_inputs():
        import jax
        import jax.numpy as jnp
        _gk = jax.random.key(seed)
        x = -7.109e-05 + 0.9999 * jax.random.normal(jax.random.fold_in(_gk, 1), (8, 32, 512, 512), jnp.float32)
        return x
    x = _rec_inputs()
    def _L0_conv_setup():
        import jax, jax.numpy as jnp
        import numpy as np
        from jax import lax
        PS = 2
        DN = ('NCHW', 'OIHW', 'NCHW')
        key = jax.random.key(seed)
        ks = jax.random.split(key, 7)
        B, C, H, W = (8, 32, 512, 512)
        return {'x': jax.random.normal(ks[0], (B, C, H, W), dtype=jnp.float32), 'mlp_w': jax.random.normal(ks[1], (1, 1), dtype=jnp.float32), 'mlp_b': jax.random.normal(ks[2], (1,), dtype=jnp.float32) * 0.1, 'conv_w': jax.random.normal(ks[3], (C, 2 * C, 1, 1), dtype=jnp.float32) * (1.0 / np.sqrt(2 * C)), 'conv_b': jax.random.normal(ks[4], (C,), dtype=jnp.float32) * 0.1, 'convout_w': jax.random.normal(ks[5], (C, 2, 7, 7), dtype=jnp.float32) * (1.0 / np.sqrt(2 * 49)), 'convout_b': jax.random.normal(ks[6], (C,), dtype=jnp.float32) * 0.1}
    _L0_conv_all = _L0_conv_setup()
    _L0_conv_in = {k: v for k, v in _L0_conv_all.items() if k in ('mlp_w', 'mlp_b', 'conv_w', 'conv_b', 'convout_w', 'convout_b', )}
    del _L0_conv_all

    def _L1_conv_setup():
        import jax, jax.numpy as jnp
        import numpy as np
        B, C_IN, H, W = (16, 32, 256, 256)
        C_OUT, KH, KW = (32, 3, 3)
        STRIDE = (1, 1)
        PADDING = (1, 1)
        key = jax.random.key(seed)
        kx, kw = jax.random.split(key)
        x = jax.random.normal(kx, (B, C_IN, H, W), dtype=jnp.float32)
        fan_in = C_IN * KH * KW
        bound = float(np.sqrt(6.0 / fan_in))
        weight = jax.random.uniform(kw, (C_OUT, C_IN, KH, KW), dtype=jnp.float32, minval=-bound, maxval=bound)
        bias = jnp.zeros((C_OUT,), dtype=jnp.float32)
        return {'x': x, 'weight': weight, 'bias': bias}
    _L1_conv_all = _L1_conv_setup()
    _L1_conv_in = {k: v for k, v in _L1_conv_all.items() if k in ('weight', 'bias', )}
    del _L1_conv_all

    return {
        "x": x,
        "L0_conv_mlp_w": _L0_conv_in["mlp_w"],
        "L0_conv_mlp_b": _L0_conv_in["mlp_b"],
        "L0_conv_conv_w": _L0_conv_in["conv_w"],
        "L0_conv_conv_b": _L0_conv_in["conv_b"],
        "L0_conv_convout_w": _L0_conv_in["convout_w"],
        "L0_conv_convout_b": _L0_conv_in["convout_b"],
        "L1_conv_weight": _L1_conv_in["weight"],
        "L1_conv_bias": _L1_conv_in["bias"],
    }

def reference(x, L0_conv_mlp_w, L0_conv_mlp_b, L0_conv_conv_w, L0_conv_conv_b, L0_conv_convout_w, L0_conv_convout_b, L1_conv_weight, L1_conv_bias):
    import jax
    import jax.numpy as jnp
    def _L0_conv_ref(x, mlp_w, mlp_b, conv_w, conv_b, convout_w, convout_b):
        import jax, jax.numpy as jnp
        import numpy as np
        from jax import lax
        PS = 2
        DN = ('NCHW', 'OIHW', 'NCHW')
        B, C, H, W = x.shape
        hn, wn = (H // PS, W // PS)
        xb = x.reshape(B, C, hn, PS, wn, PS)
        m = jnp.max(xb, axis=(3, 5))
        a = jnp.mean(xb, axis=(3, 5))
        gate = jax.nn.sigmoid((m + a) * mlp_w[0, 0] + 2.0 * mlp_b[0])
        product = (xb * gate[:, :, :, None, :, None]).reshape(B, C, H, W)
        cat = jnp.concatenate([product, x], axis=1)
        out = lax.conv_general_dilated(cat, conv_w, (1, 1), 'SAME', dimension_numbers=DN) + conv_b[None, :, None, None]
        fs = out
        cm = jnp.max(out, axis=1, keepdims=True)
        ca = jnp.mean(out, axis=1, keepdims=True)
        att = lax.conv_general_dilated(jnp.concatenate([cm, ca], axis=1), convout_w, (1, 1), 'SAME', dimension_numbers=DN)
        att = att + convout_b[None, :, None, None]
        return jax.nn.sigmoid(att) * fs

    def _L1_conv_ref(x, weight, bias):
        import jax, jax.numpy as jnp
        import numpy as np
        B, C_IN, H, W = (16, 32, 256, 256)
        C_OUT, KH, KW = (32, 3, 3)
        STRIDE = (1, 1)
        PADDING = (1, 1)
        out = jax.lax.conv_general_dilated(x, weight, window_strides=STRIDE, padding=[(PADDING[0], PADDING[0]), (PADDING[1], PADDING[1])], dimension_numbers=('NCHW', 'OIHW', 'NCHW'))
        return out + bias[None, :, None, None]

    def _gn(v, G=16, eps=1e-5):
        B_, C_, H_, W_ = v.shape
        g = v.reshape(B_, G, C_ // G, H_, W_)
        m = jnp.mean(g, axis=(2, 3, 4), keepdims=True)
        s = jnp.var(g, axis=(2, 3, 4), keepdims=True)
        return ((g - m) / jnp.sqrt(s + eps)).reshape(v.shape)

    def _ln_c(v, eps=1e-6):
        m = jnp.mean(v, axis=1, keepdims=True)
        s = jnp.var(v, axis=1, keepdims=True)
        return (v - m) / jnp.sqrt(s + eps)

    def _ln_t(v, eps=1e-5):
        m = jnp.mean(v, axis=-1, keepdims=True)
        s = jnp.var(v, axis=-1, keepdims=True)
        return (v - m) / jnp.sqrt(s + eps)

    def _to_tokens(v):
        B_, C_, H_, W_ = v.shape
        return v.reshape(B_, C_, H_ * W_).transpose(0, 2, 1)
    def _from_tokens(t, like):
        B_, C_, H_, W_ = like.shape
        return t.transpose(0, 2, 1).reshape(B_, C_, H_, W_)

    x = x + _L0_conv_ref(_gn(x), L0_conv_mlp_w, L0_conv_mlp_b, L0_conv_conv_w, L0_conv_conv_b, L0_conv_convout_w, L0_conv_convout_b)
    x = x + _L1_conv_ref(_gn(x), L1_conv_weight, L1_conv_bias)
    return x


_drawn_inputs = setup_inputs


def setup_inputs(seed=0):
    import zlib

    import numpy as np

    out = dict(_drawn_inputs(seed))
    spreads = {'L1_conv_bias': (0.0, 0.1)}
    factors = {'L0_conv_convout_b': 3.264}
    for name, (base, spread) in spreads.items():
        noise = np.random.default_rng([zlib.crc32(name.encode()), seed]).standard_normal(out[name].shape)
        drawn = base * np.exp(spread * noise) if base else spread * noise
        out[name] = jnp.asarray(drawn.astype(out[name].dtype))
    for name, factor in factors.items():
        out[name] = (out[name] * factor).astype(out[name].dtype)
    return out
```

```python
from contextlib import ExitStack

import concourse.bass as bass
from concourse import mybir

ALU = mybir.AluOpType
ACT = mybir.ActivationFunctionType
F32 = mybir.dt.float32
AX_X = mybir.AxisListType.X

P = 128
EPS = 1e-5
SUB = 4
ROWS = 8
KW7 = 7
WIN7 = ROWS + KW7 - 1
DXA = 4
XRING = 12
LRING = 4


class Step:

    def __init__(self, turn, place, unroll, total):
        self.turn, self.place, self.unroll, self.total = turn, place, unroll, total

    def number(self):
        return self.unroll * self.turn + self.place

    def back(self, lag):
        turn, place = self.turn, self.place - lag
        while place < 0:
            turn, place = turn - 1, place + self.unroll
        return Step(turn, place, self.unroll, self.total)

    def fixed(self):
        return isinstance(self.turn, int)

    def after(self, steps):
        return not self.fixed() or self.number() >= steps

    def exists(self):
        return not self.fixed() or 0 <= self.number() < self.total


def run_steps(eng, unroll, total, most_lag, body):
    for n in range(unroll):
        body(Step(0, n, unroll, total))
    turns = total // unroll
    if turns > 1:
        with eng.Fori(1, turns) as i:
            for j in range(unroll):
                body(Step(i, j, unroll, total))
    for n in range(turns * unroll, total + most_lag):
        body(Step(n // unroll, n % unroll, unroll, total))


def count(b, step, ago=0):
    return b * step.total + step.number() + (1 - ago)


def slot_count(b, step, ring, ago=0):
    slot = step.place % ring
    per_turn = step.unroll // ring
    per_batch = len(range(slot, step.total, ring))
    uses = step.turn * per_turn + step.place // ring + 1 - ago
    return (b * per_batch + uses) * 16


def build(nc, x, mlp_w, mlp_b, conv_wt, conv_b, att_wt, att_b, c3_wt, c3_b,
          ident_c, group_c, chscale_c, icentre_c, out):
    B, C, H, W = x.shape
    assert C * SUB == P and 2 * W == 1024
    TILES = H // ROWS
    N = 2 * W
    HW2 = W // 2
    CH = W // P
    SROW = W + KW7 + 1
    SH = H + KW7 - 1
    KA, KB = WIN7 * 2 * DXA, WIN7 * 2 * (KW7 - DXA)
    YH = H + 2
    CHUNKS = TILES
    T3 = ROWS // 2
    W3 = W + 2

    with ExitStack() as ctx:
        def sb(name, shape):
            return ctx.enter_context(nc.sbuf_tensor(name, shape, F32))

        def sem(name):
            return ctx.enter_context(nc.semaphore(name))

        def sems(name, n):
            return [sem(f"{name}{i}") for i in range(n)]

        pooled_d = nc.dram_tensor("pooled_scratch", (SH, 2, SROW), F32, kind="Internal").ap()
        y_d = nc.dram_tensor("y_scratch", (C, YH, W), F32, kind="Internal").ap()

        ps = ctx.enter_context(nc.psum_tensor("ps", [P, 8, 512], F32))
        ps_mix = ps[:, 0:2, :]
        ps_tr = ps[:, 2:4, :]
        ps_att = ps[:, 4:6, :]
        ps_st = ps[:, 6, 0:P]
        ps_par = ps[:, 7, 0:4]

        ident = sb("ident", [P, P])
        group = sb("group", [P, P])
        chscale = sb("chscale", [P, 2])
        icentre = sb("icentre", [P, 64])
        stage_mix = sb("stage_mix", [P, 2, SUB, C])
        mix_w = sb("mix_w", [P, 2, P])
        mix_s = sb("mix_s", [P, 2, P])
        stage_a = sb("stage_a", [KA, 2, SUB, C])
        stage_b = sb("stage_b", [KB, 2, SUB, C])
        att_wa = sb("att_wa", [KA, 2, P])
        att_wb = sb("att_wb", [KB, 2, P])
        stage_3 = sb("stage_3", [P, 3, 2, C])
        c3_w = sb("c3_w", [P, 3, 64])
        c3_s = sb("c3_s", [P, 3, 64])
        c3_f = sb("c3_f", [P, 64])
        zeros = sb("zeros", [P, SROW])
        wcol = sb("wcol", [P, 1])
        twob = sb("twob", [P, 1])
        mixb = sb("mixb", [P, 1])
        attb = sb("attb", [P, 1])
        c3b = sb("c3b", [P, 1])
        px = sb("px", [P, 16])
        py = sb("py", [P, 16])

        idle = sb("idle", [P, 1])

        xt = sb("xt", [P, XRING, N])
        mixed_win = sb("mixed_win", [P, XRING * N])
        mixed = mixed_win[:, :].rearrange("p (a n) -> p a n", n=N)
        win = mixed_win[:, 0:LRING * T3 * W3].rearrange("p (a t w) -> p a t w", t=T3, w=W3)
        hmax = sb("hmax", [P, 2, HW2])
        hsum = sb("hsum", [P, 2, HW2])
        vsum = sb("vsum", [P, W])
        vmax = sb("vmax", [P, W])
        gate = sb("gate", [P, 2, HW2])
        prod = sb("prod", [P, 2, N])
        sig = sb("sig", [P, 2, N])
        stat = sb("stat", [P, 2, P])
        statT = sb("statT", [64, 3, P])
        ima = sb("ima", [KA, 3, W])
        imb = sb("imb", [KB, 3, W])
        bnx = sb("bnx", [P, TILES, 2, 6])
        bny = sb("bny", [P, TILES, 2, 6])
        xa = sb("xa", [P, LRING, N])
        ot = sb("ot", [P, LRING, 2, W])
        mrow = sb("mrow", [P, W])

        consts = sem("consts")
        zeros_set = sem("zeros_set")
        stage_zero = sem("stage_zero")
        zeroed = sem("zeroed")
        weights_in = sem("weights_in")
        weights_set = sem("weights_set")
        xa_in = sems("xa_in", LRING)
        bnx_done = sem("bnx_done")
        small = sem("small")
        agg_ready = sem("agg_ready")
        par_mm = sem("par_mm")
        root_asked = sem("root_asked")
        root_done = sem("root_done")
        x_ready = sem("x_ready")
        y_ready = sem("y_ready")
        pad_rows = sem("pad_rows")
        between = sem("between")
        x_in = sems("x_in", XRING)
        vmax_done = sem("vmax_done")
        hmax_done = sem("hmax_done")
        vsum_done = sem("vsum_done")
        hsum_done = sem("hsum_done")
        garg_done = sem("garg_done")
        gate_done = sem("gate_done")
        prod_done = sem("prod_done")
        mix_done = sem("mix_done")
        mixed_done = sem("mixed_done")
        tr_done = sem("tr_done")
        stat_done = sem("stat_done")
        st_done = sem("st_done")
        statT_done = sem("statT_done")
        pooled_out = sems("pooled_out", 3)
        im_in = sems("im_in", 3)
        att_done = sem("att_done")
        sig_done = sem("sig_done")
        gated = sem("gated")
        y_done = sem("y_done")
        bny_done = sem("bny_done")
        y_out = sems("y_out", XRING)
        win_in = sems("win_in", LRING)
        c3_done = sems("c3_done", 2)
        out_lo = sem("out_lo")
        out_hi = sem("out_hi")
        o_out = sems("o_out", LRING)

        def x_tile_at(b, k):
            return b * (C * H * W) + k * (ROWS * W)

        def x_tile(at):
            return bass.AP(x.tensor, at, [[H * W, C], [N, SUB], [1, N]])

        def y_tile(k):
            return bass.AP(y_d.tensor, k * (ROWS * W) + W, [[YH * W, C], [N, SUB], [1, N]])

        def settled(eng, value):
            return value if isinstance(value, int) else eng.snap(value)

        def taps(at, dxn):
            return bass.AP(pooled_d.tensor, at,
                           [[2 * SROW, WIN7], [SROW, 2], [1, dxn], [1, W]])

        def y_window(at):
            return bass.AP(y_d.tensor, at, [[YH * W, C], [W, 4], [1, W]])

        def out_rows(b, q, g, u):
            return bass.AP(out.tensor, b * (C * H * W) + q * (ROWS * W) + (4 * g + 2 * u) * W,
                           [[H * W, C], [W, 2], [1, W]])

        def pooled_rows(k, a):
            return bass.AP(pooled_d.tensor, k * (ROWS * 2 * SROW) + 3 * (2 * SROW) + a * SROW + 3,
                           [[2 * SROW, ROWS], [1, W]])

        LAG_GATED, LAG_ADD, LAG_Y = 8, 9, 10

        block = ctx.enter_context(nc.Block())

        @block.sync
        def _(sp):
            small_loads = [
                (ident[:, :], ident_c), (group[:, :], group_c), (chscale[:, :], chscale_c),
                (icentre[:, :], icentre_c),
                (wcol[:, :], bass.AP(mlp_w.tensor, 0, [[0, P], [1, 1]])),
                (twob[:, :], bass.AP(mlp_b.tensor, 0, [[0, P], [1, 1]])),
                (mixb[:, :], bass.AP(conv_b.tensor, 0, [[1, C], [0, SUB], [1, 1]])),
                (attb[:, :], bass.AP(att_b.tensor, 0, [[1, C], [0, SUB], [1, 1]])),
                (c3b[0:64, :], bass.AP(c3_b.tensor, 0, [[1, C], [0, 2], [1, 1]])),
                (c3b[64:P, :], bass.AP(c3_b.tensor, 0, [[1, C], [0, 2], [1, 1]])),
            ]
            for dst, src in small_loads:
                sp.dma_start(dst, src).then_inc(consts, 16)
            sp.wait_ge(stage_zero, 4)
            n = 0
            for s in range(SUB):
                for part in range(2):
                    sp.dma_start(stage_mix[s::SUB, part, s, :], conv_wt[part * C:(part + 1) * C, :])\
                        .then_inc(weights_in, 16)
                    n += 1
                for r in range(2):
                    row = 2 * s + r
                    for stage, dx0, dxn in ((stage_a, 0, DXA), (stage_b, DXA, KW7 - DXA)):
                        sp.dma_start(stage[row * 2 * dxn:(row + KW7) * 2 * dxn, r, s, :],
                                     att_wt[:, dx0:dx0 + dxn, :]).then_inc(weights_in, 16)
                        n += 1
            for r in range(2):
                for dy in range(3):
                    sp.dma_start(stage_3[r + dy::4, :, r, :], c3_wt[dy].rearrange("d c o -> c d o"))\
                        .then_inc(weights_in, 16)
                    n += 1
            assert n == WEIGHT_LOADS
            sp.wait_ge(zeros_set, 2)
            rows = pooled_d.rearrange("h c w -> (h c) w")
            for at in range(0, 2 * SH, P):
                m = min(P, 2 * SH - at)
                sp.dma_start(rows[at:at + m, :], zeros[0:m, :]).then_inc(zeroed, 16)
            sp.wait_ge(zeroed, 16 * -(-2 * SH // P))

            def load_stat(b, step):
                if not step.exists():
                    return
                slot = step.place % LRING
                if step.after(LRING):
                    counted = settled(sp, count(b, step, LRING))
                at = settled(sp, x_tile_at(b, step.number()))
                if step.after(LRING):
                    sp.wait_ge(bnx_done, counted)
                sp.dma_start(xa[:, slot, :], x_tile(at)).then_inc(xa_in[slot], 16)

            def layer0(b):
                def body(step):
                    tile = step.back(8)
                    if tile.exists():
                        slot = tile.place % 3
                        nxt = step.back(7)
                        if nxt.exists():
                            written = settled(sp, 2 * slot_count(b, nxt, 3))
                        if tile.after(3):
                            used = settled(sp, count(b, tile, 3))
                        at = [settled(sp, tile.number() * (ROWS * 2 * SROW) + dx0) for dx0 in (0, DXA)]
                        if nxt.exists():
                            sp.wait_ge(pooled_out[nxt.place % 3], written)
                            sp.sem_inc(between, 1)
                        if tile.after(3):
                            sp.wait_ge(att_done, used)
                        sp.dma_start(ima[:, slot, :], taps(at[0], DXA)).then_inc(im_in[slot], 16)
                        sp.dma_start(imb[:, slot, :], taps(at[1], KW7 - DXA)).then_inc(im_in[slot], 16)
                    if step.exists():
                        slot = step.place % XRING
                        if step.after(XRING):
                            stored = settled(sp, slot_count(b, step, XRING, 1))
                            counted = settled(sp, count(b, step, XRING))
                        at = settled(sp, x_tile_at(b, step.number()))
                        if step.after(XRING):
                            sp.wait_ge(y_out[slot], stored)
                            sp.sem_inc(between, 1)
                            sp.wait_ge(bny_done, counted)
                        sp.dma_start(xt[:, slot, :], x_tile(at)).then_inc(x_in[slot], 16)
                run_steps(sp, XRING, TILES, 8, body)

            def layer1(b, with_stats):
                stored = [settled(sp, (b + 1) * (16 * len(range(slot, TILES, XRING))))
                          for slot in range(XRING)]
                ready = settled(sp, b + 1)
                padded = settled(sp, b * 32 + 32)
                for slot in range(XRING):
                    sp.wait_ge(y_out[slot], stored[slot])
                    sp.sem_inc(between, 1)
                sp.wait_ge(y_ready, ready)
                sp.dma_start(y_d[:, 0, :], mrow[::SUB, :]).then_inc(pad_rows, 16)
                sp.dma_start(y_d[:, YH - 1, :], mrow[::SUB, :]).then_inc(pad_rows, 16)
                sp.wait_ge(pad_rows, padded)
                sp.sem_inc(between, 1)

                def body(step):
                    slot = step.place % LRING
                    if step.after(LRING):
                        used = settled(sp, count(b, step, LRING))
                    at = [settled(sp, step.number() * (ROWS * W) + t * (2 * W)) for t in range(T3)]
                    if step.after(LRING):
                        sp.wait_ge(c3_done[1], used)
                    for t in range(T3):
                        sp.dma_start(win[:, slot, t, 1:1 + W], y_window(at[t]))\
                            .then_inc(win_in[slot], 16)
                    if with_stats:
                        load_stat(b + 1, step)
                run_steps(sp, LRING, CHUNKS, 0, body)

            run_steps(sp, LRING, CHUNKS, 0, lambda step: load_stat(0, step))
            with sp.Fori(0, B - 1) as b:
                layer0(b)
                layer1(b, True)
            layer0(B - 1)
            layer1(B - 1, False)

        @block.gpsimd
        def _(pool):
            def layer0(b):
                def body(step):
                    if step.exists():
                        slot, two = step.place % XRING, step.place % 2
                        pool.wait_ge(x_in[slot], slot_count(b, step, XRING))
                        pool.tensor_tensor(vsum[:, :], xt[:, slot, 0:W], xt[:, slot, W:N], ALU.add)\
                            .then_inc(vsum_done, 1)
                        pool.wait_ge(vsum_done, count(b, step))
                        if step.after(2):
                            pool.wait_ge(garg_done, count(b, step, 2))
                        v = vsum[:, :].rearrange("p (j t) -> p j t", t=2)
                        pool.tensor_tensor(hsum[:, two, :], v[:, :, 0], v[:, :, 1], ALU.add)\
                            .then_inc(hsum_done, 1)
                        pool.wait_ge(hsum_done, count(b, step))
                    tile = step.back(LAG_ADD)
                    if tile.exists():
                        slot = tile.place % XRING
                        pool.wait_ge(gated, count(b, tile))
                        pool.tensor_tensor(xt[:, slot, :], xt[:, slot, :], mixed[:, tile.place % XRING, :],
                                           ALU.add).then_inc(y_done, 1)
                run_steps(pool, XRING, TILES, LAG_ADD, body)

            with pool.Fori(0, B) as b:
                layer0(b)

        @block.scalar
        def _(act):
            def root(turn, par):
                act.wait_ge(root_asked, turn + 1)
                act.activation(par[:, 12:13], par[:, 11:12], ACT.Sqrt).then_inc(root_done, 1)

            def layer0(b):
                root(2 * b, px)
                act.wait_ge(x_ready, b + 1)

                def body(step):
                    tile = step.back(LAG_Y)
                    if tile.exists():
                        slot = tile.place % XRING
                        act.wait_ge(y_done, count(b, tile))
                        act.dma_start(y_tile(tile.number()), xt[:, slot, :]).then_inc(y_out[slot], 16)
                    if step.exists():
                        two = step.place % 2
                        act.wait_ge(garg_done, count(b, step))
                        if step.after(2):
                            act.wait_ge(prod_done, count(b, step, 2))
                        act.activation(gate[:, two, :], hmax[:, two, :], ACT.Sigmoid,
                                       bias=px[:, 7:8], scale=px[:, 6:7]).then_inc(gate_done, 1)
                    tile = step.back(2)
                    if tile.exists():
                        slot = tile.place % XRING
                        act.wait_ge(mix_done, count(b, tile))
                        if tile.after(XRING - 2):
                            act.wait_ge(y_done, count(b, tile, XRING - 2))
                        act.activation(mixed[:, slot, :], ps_mix.rearrange("p a n -> p (a n)"),
                                       ACT.Identity, bias=px[:, 9:10]).then_inc(mixed_done, 1)
                    tile = step.back(4)
                    if tile.exists():
                        slot = tile.place % 3
                        act.wait_ge(st_done, count(b, tile))
                        if tile.after(3):
                            act.wait_ge(pooled_out[slot], 2 * slot_count(b, tile, 3, 1))
                        act.activation(statT[:, slot, :], ps_st[0:64, :], ACT.Copy).then_inc(statT_done, 1)
                        act.wait_ge(statT_done, count(b, tile))
                        for a in range(2):
                            act.dma_start(pooled_rows(tile.number(), a), statT[32 * a:32 * a + 32, slot, :])\
                                .then_inc(pooled_out[slot], 16)
                    tile = step.back(7)
                    if tile.exists():
                        act.wait_ge(att_done, count(b, tile))
                        if tile.after(2):
                            act.wait_ge(gated, count(b, tile, 2))
                        act.activation(sig[:, tile.place % 2, :], ps_att.rearrange("p a n -> p (a n)"),
                                       ACT.Sigmoid, bias=attb[:, :]).then_inc(sig_done, 1)
                run_steps(act, XRING, TILES, LAG_Y, body)

            def layer1(b):
                root(2 * b + 1, py)
                act.wait_ge(y_ready, b + 1)

                def body(step):
                    if step.exists():
                        slot = step.place % LRING
                        act.wait_ge(c3_done[0], count(b, step))
                        if step.after(LRING):
                            act.wait_ge(o_out[slot], 4 * slot_count(b, step, LRING, 1))
                        act.activation(ot[:, slot, 0, :], ps[:, step.place % 2 * 2, :], ACT.Identity,
                                       bias=py[:, 9:10]).then_inc(out_lo, 1)
                    chunk = step.back(1)
                    if chunk.exists():
                        slot = chunk.place % LRING
                        for u in range(2):
                            act.wait_ge((out_lo, out_hi)[u], count(b, chunk))
                            for g in range(2):
                                act.dma_start(out_rows(b, chunk.number(), g, u),
                                              ot[64 * g:64 * g + 64, slot, u, :]).then_inc(o_out[slot], 16)
                run_steps(act, LRING, CHUNKS, 1, body)
                for slot in range(LRING):
                    act.wait_ge(o_out[slot], (b + 1) * (64 * CHUNKS // LRING))

            act.wait_ge(consts, 16 * 10)
            with act.Fori(0, B) as b:
                layer0(b)
                layer1(b)

        @block.tensor
        def _(pe):
            def parameters(b, par, base, fold):
                at = 6 * b + base
                pe.wait_ge(agg_ready, at + 1)
                pe.matmul(ps_par[:, 0:1], group[:, :], par[:, 0:1], start=True, stop=True).then_inc(par_mm, 1)
                pe.wait_ge(agg_ready, at + 2)
                pe.matmul(ps_par[:, 1:2], group[:, :], par[:, 3:4], start=True, stop=True).then_inc(par_mm, 1)
                pe.wait_ge(agg_ready, at + 3)
                fold().then_inc(par_mm, 1)

            def fold_x():
                return pe.matmul(ps_par[:, 2:3], mix_s[:, 1, :], px[:, 4:5], start=True, stop=True)

            def fold_y():
                for g in range(2):
                    for dx in range(3):
                        last = pe.matmul(ps_par[64 * g:64 * g + 64, 2:3], c3_s[:, dx, :], py[:, 4:5],
                                         start=(dx == 0), stop=(dx == 2))
                return last

            def layer0(b):
                pe.wait_ge(x_ready, b + 1)

                def body(step):
                    if step.exists():
                        slot, two = step.place % XRING, step.place % 2
                        pe.wait_ge(x_in[slot], slot_count(b, step, XRING))
                        if step.after(1):
                            pe.wait_ge(mixed_done, count(b, step, 1))
                        for r in range(2):
                            pe.matmul(ps_mix[:, r, :], mix_s[:, 1, :], xt[:, slot, r * W:(r + 1) * W],
                                      start=True, stop=False)
                        pe.wait_ge(prod_done, count(b, step))
                        for r in range(2):
                            last = pe.matmul(ps_mix[:, r, :], mix_s[:, 0, :], prod[:, two, r * W:(r + 1) * W],
                                             start=False, stop=True)
                        last.then_inc(mix_done, 1)
                    tile = step.back(5)
                    if tile.exists():
                        slot = tile.place % 3
                        pe.wait_ge(im_in[slot], 2 * slot_count(b, tile, 3))
                        if tile.after(1):
                            pe.wait_ge(sig_done, count(b, tile, 1))
                        for r in range(2):
                            pe.matmul(ps_att[:, r, :], att_wa[:, r, :], ima[:, slot, :], start=True, stop=False)
                            last = pe.matmul(ps_att[:, r, :], att_wb[:, r, :], imb[:, slot, :],
                                             start=False, stop=True)
                        last.then_inc(att_done, 1)
                    tile = step.back(2)
                    if tile.exists():
                        pe.wait_ge(stat_done, count(b, tile))
                        if tile.after(1):
                            pe.wait_ge(statT_done, count(b, tile, 1))
                        pe.transpose(ps_st, stat[:, tile.place % 2, :], ident[:, :])\
                            .then_inc(st_done, 1)
                    if step.exists():
                        slot = step.place % XRING
                        pe.wait_ge(mixed_done, count(b, step))
                        if step.after(1):
                            pe.wait_ge(stat_done, count(b, step, 1))
                        for n in range(2 * CH):
                            last = pe.transpose(ps_tr[:, n // CH, n % CH * P:n % CH * P + P],
                                                mixed[:, slot, n * P:(n + 1) * P], ident[:, :])
                        last.then_inc(tr_done, 1)
                run_steps(pe, XRING, TILES, 5, body)

            def layer1(b):
                pe.wait_ge(y_ready, b + 1)
                pe.wait_ge(sig_done, (b + 1) * TILES)

                def body(step):
                    slot = step.place % LRING
                    pe.wait_ge(win_in[slot], T3 * slot_count(b, step, LRING))
                    for u in range(2):
                        bank = ps[:, step.place % 2 * 2 + u, :]
                        if step.after(2):
                            pe.wait_ge((out_lo, out_hi)[u], count(b, step, 2))
                        for n, dx in enumerate((1, 0, 2)):
                            w = c3_f[:, :] if dx == 1 else c3_s[:, dx, :]
                            for g in range(2):
                                last = pe.matmul(bank[64 * g:64 * g + 64, :], w,
                                                 win[:, slot, 2 * g + u, dx:dx + W],
                                                 start=(n == 0), stop=(n == 2))
                        last.then_inc(c3_done[u], 1)
                run_steps(pe, LRING, CHUNKS, 0, body)

            pe.wait_ge(consts, 16 * 10)
            pe.wait_ge(weights_set, 5)
            with pe.Fori(0, B) as b:
                parameters(b, px, 0, fold_x)
                layer0(b)
                parameters(b, py, 3, fold_y)
                layer1(b)

        @block.vector
        def _(dve):
            SMALL_X, SMALL_Y = 12, 9

            for n, stage in enumerate((stage_mix, stage_a, stage_b, stage_3)):
                dve.memset(stage[:, :], 0.0).then_inc(stage_zero, 1)
            dve.memset(zeros[:, :], 0.0).then_inc(zeros_set, 1)
            dve.memset(stat[:, :, :], 0.0).then_inc(zeros_set, 1)
            dve.wait_ge(consts, 16 * 10)
            dve.wait_ge(weights_in, 16 * WEIGHT_LOADS)
            dve.tensor_copy(mix_w[:, :, :].rearrange("p a (o s) -> p a s o", s=SUB), stage_mix[:, :, :, :])\
                .then_inc(weights_set, 1)
            for stage, dst, col, k in ((stage_a, att_wa, 0, KA), (stage_b, att_wb, 1, KB)):
                dve.tensor_scalar(dst[:, :, :].rearrange("p a (o s) -> p a s o", s=SUB), stage[:, :, :, :],
                                  chscale[0:k, col:col + 1], None, ALU.mult).then_inc(weights_set, 1)
            dve.tensor_copy(c3_w[:, :, :].rearrange("p a (o r) -> p a r o", r=2), stage_3[:, :, :, :])\
                .then_inc(weights_set, 1)
            dve.tensor_scalar(mrow[:, 0:1], twob[:, :], 2.0, None, ALU.mult).then_inc(weights_set, 1)
            dve.wait_ge(weights_set, 5)
            dve.tensor_copy(twob[:, :], mrow[:, 0:1]).then_inc(weights_set, 1)
            dve.wait_ge(weights_set, 6)

            def count_x(b, step):
                slot = step.place % LRING
                dve.wait_ge(xa_in[slot], slot_count(b, step, LRING))
                n = step.number()
                for r in range(2):
                    last = dve.bn_stats(bnx_at(step, r), xa[:, slot, r * W:(r + 1) * W])
                last.then_inc(bnx_done, 1)

            def bnx_at(step, r):
                return bnx[:, bass.ds(step.number(), 1), r, :].rearrange("p a n -> p (a n)")

            def bny_at(step, r):
                return bny[:, bass.ds(step.number(), 1), r, :].rearrange("p a n -> p (a n)")

            def norm_parameters(b, par, stats, turn, chain):
                dve.memset(idle[:, :], 0.0)
                chain(dve.bn_aggr(par[:, 0:2], stats[:, :, :, :].rearrange("p a b c -> p (a b c)")))
                dve.sem_inc(agg_ready, 1)
                dve.wait_ge(par_mm, 3 * turn + 1)
                chain(dve.tensor_scalar(par[:, 2:3], par[:, 0:1], ps_par[:, 0:1], None, ALU.subtract))
                dve.tensor_copy(par[:, 4:5], ps_par[:, 0:1]).then_inc(small, 1)
                chain.at += 1
                dve.scalar_tensor_tensor(out=par[:, 3:4], in0=par[:, 2:3], scalar=par[:, 2:3], in1=par[:, 1:2],
                                         op0=ALU.mult, op1=ALU.add).then_inc(agg_ready, 1)
                dve.wait_ge(par_mm, 3 * turn + 2)
                chain(dve.tensor_scalar(par[:, 11:12], ps_par[:, 1:2], EPS, None, ALU.add))
                dve.sem_inc(root_asked, 1)
                dve.wait_ge(root_done, turn + 1)
                chain(dve.reciprocal(par[:, 13:14], par[:, 12:13]))
                chain(dve.tensor_scalar(par[:, 14:15], par[:, 13:14], par[:, 13:14], par[:, 11:12],
                                        ALU.mult, ALU.mult))
                chain(dve.tensor_scalar(par[:, 15:16], par[:, 14:15], -0.5, 1.5, ALU.mult, ALU.add))
                chain(dve.tensor_scalar(par[:, 5:6], par[:, 15:16], par[:, 13:14], None, ALU.mult))

            class Chain:

                def __init__(self, base):
                    self.base, self.at = base, 0

                def __call__(self, ins):
                    self.at += 1
                    ins.then_inc(small, 1)
                    dve.wait_ge(small, self.base + self.at)

            def x_parameters(b):
                chain = Chain(b * (SMALL_X + SMALL_Y))
                dve.wait_ge(bnx_done, (b + 1) * CHUNKS)
                norm_parameters(b, px, bnx, 2 * b, chain)
                chain(dve.tensor_scalar(px[:, 6:7], px[:, 5:6], wcol[:, 0:1], None, ALU.mult))
                chain(dve.tensor_scalar(px[:, 8:9], px[:, 4:5], -1.0, None, ALU.mult))
                chain(dve.tensor_scalar(px[:, 10:11], px[:, 8:9], px[:, 6:7], 2.0, ALU.mult, ALU.mult))
                chain(dve.tensor_scalar(px[:, 7:8], px[:, 10:11], twob[:, 0:1], None, ALU.add))
                dve.tensor_scalar(mix_s[:, :, :], mix_w[:, :, :], px[:, 5:6], None, ALU.mult)\
                    .then_inc(agg_ready, 1)
                dve.wait_ge(par_mm, 6 * b + 3)
                dve.scalar_tensor_tensor(out=px[:, 9:10], in0=ps_par[:, 2:3], scalar=-1.0, in1=mixb[:, :],
                                         op0=ALU.mult, op1=ALU.add).then_inc(x_ready, 1)
                assert chain.at == SMALL_X

            def y_parameters(b):
                chain = Chain(b * (SMALL_X + SMALL_Y) + SMALL_X)
                dve.wait_ge(bny_done, (b + 1) * TILES)
                norm_parameters(b, py, bny, 2 * b + 1, chain)
                dve.tensor_scalar(c3_s[:, :, :], c3_w[:, :, :], py[:, 5:6], None, ALU.mult)\
                    .then_inc(agg_ready, 1)
                dve.wait_ge(agg_ready, 6 * b + 6)
                dve.tensor_tensor(c3_f[:, :], c3_s[:, 1, :], icentre[:, :], ALU.add)
                dve.tensor_scalar(mrow[:, :], zeros[:, 0:W], py[:, 4:5], None, ALU.add)
                for slot in range(LRING):
                    dve.tensor_scalar(win[:, slot, :, 0:W3:W3 - 1],
                                      zeros[:, 0:2 * T3].rearrange("p (a b) -> p a b", b=2),
                                      py[:, 4:5], None, ALU.add)
                dve.wait_ge(par_mm, 6 * b + 6)
                chain(dve.scalar_tensor_tensor(out=py[:, 9:10], in0=ps_par[:, 2:3], scalar=-1.0, in1=c3b[:, :],
                                               op0=ALU.mult, op1=ALU.add))
                dve.sem_inc(y_ready, 1)
                assert chain.at == SMALL_Y

            def layer0(b):
                dve.wait_ge(x_ready, b + 1)

                def body(step):
                    tile = step.back(3)
                    if tile.exists():
                        two = tile.place % 2
                        dve.wait_ge(tr_done, count(b, tile))
                        if tile.after(2):
                            dve.wait_ge(st_done, count(b, tile, 2))
                        src = ps_tr.rearrange("p a (n c s) -> p s (a n) c", c=C, s=SUB)
                        dst = stat[:, two, 0:64].rearrange("p (t s n) -> p t s n", s=SUB, t=2)
                        dve.tensor_reduce(dst[:, 0], src, AX_X, ALU.max)
                        dve.tensor_reduce(dst[:, 1], src, AX_X, ALU.add).then_inc(stat_done, 1)
                    if step.exists():
                        slot = step.place % XRING
                        dve.wait_ge(x_in[slot], slot_count(b, step, XRING))
                        if step.after(1):
                            dve.wait_ge(hmax_done, count(b, step, 1))
                        dve.tensor_tensor(vmax[:, :], xt[:, slot, 0:W], xt[:, slot, W:N], ALU.max)\
                            .then_inc(vmax_done, 1)
                    if step.exists():
                        two = step.place % 2
                        dve.wait_ge(vmax_done, count(b, step))
                        if step.after(2):
                            dve.wait_ge(gate_done, count(b, step, 2))
                        v = vmax[:, :].rearrange("p (j t) -> p j t", t=2)
                        dve.tensor_tensor(hmax[:, two, :], v[:, :, 0], v[:, :, 1], ALU.max)\
                            .then_inc(hmax_done, 1)
                    tile = step.back(1)
                    if tile.exists():
                        slot, two = tile.place % XRING, tile.place % 2
                        dve.wait_ge(gate_done, count(b, tile))
                        if tile.after(2):
                            dve.wait_ge(mix_done, count(b, tile, 2))
                        wide = gate[:, two, :].rearrange("p (j t) -> p j t", t=1).broadcast_to([P, HW2, 2])
                        for r in range(2):
                            row = slice(r * W, (r + 1) * W)
                            last = dve.scalar_tensor_tensor(
                                out=prod[:, two, row].rearrange("p (j t) -> p j t", t=2),
                                in0=xt[:, slot, row].rearrange("p (j t) -> p j t", t=2),
                                scalar=px[:, 8:9], in1=wide, op0=ALU.add, op1=ALU.mult)
                        last.then_inc(prod_done, 1)
                    if step.exists():
                        two = step.place % 2
                        dve.wait_ge(hsum_done, count(b, step))
                        dve.wait_ge(hmax_done, count(b, step))
                        dve.scalar_tensor_tensor(out=hmax[:, two, :], in0=hsum[:, two, :], scalar=0.25,
                                                 in1=hmax[:, two, :], op0=ALU.mult, op1=ALU.add)\
                            .then_inc(garg_done, 1)
                    tile = step.back(LAG_GATED)
                    if tile.exists():
                        slot = tile.place % XRING
                        dve.wait_ge(sig_done, count(b, tile))
                        dve.wait_ge(tr_done, count(b, tile))
                        dve.tensor_tensor(mixed[:, slot, :], mixed[:, slot, :], sig[:, tile.place % 2, :],
                                          ALU.mult).then_inc(gated, 1)
                    tile = step.back(LAG_Y)
                    if tile.exists():
                        slot = tile.place % XRING
                        dve.wait_ge(y_done, count(b, tile))
                        for r in range(2):
                            last = dve.bn_stats(bny_at(tile, r), xt[:, slot, r * W:(r + 1) * W])
                        last.then_inc(bny_done, 1)
                run_steps(dve, XRING, TILES, LAG_Y, body)

            def layer1(b, with_stats):
                def body(step):
                    slot = step.place % LRING
                    if with_stats:
                        count_x(b + 1, step)
                    dve.wait_ge(c3_done[1], count(b, step))
                    if step.after(LRING):
                        dve.wait_ge(o_out[slot], 4 * slot_count(b, step, LRING, 1))
                    dve.tensor_scalar(ot[:, slot, 1, :], ps[:, step.place % 2 * 2 + 1, :], py[:, 9:10], None,
                                      ALU.add).then_inc(out_hi, 1)
                run_steps(dve, LRING, CHUNKS, 0, body)

            run_steps(dve, LRING, CHUNKS, 0, lambda step: count_x(0, step))
            with dve.Fori(0, B - 1) as b:
                x_parameters(b)
                layer0(b)
                y_parameters(b)
                layer1(b, True)
            x_parameters(B - 1)
            layer0(B - 1)
            y_parameters(B - 1)
            layer1(B - 1, False)


WEIGHT_LOADS = SUB * (2 + 4) + 6


def kernel(x, L0_conv_mlp_w, L0_conv_mlp_b, L0_conv_conv_w, L0_conv_conv_b, L0_conv_convout_w,
           L0_conv_convout_b, L1_conv_weight, L1_conv_bias):
    import numpy as np
    import concourse.bacc as bacc
    from concourse.bass_utils import run_bass_kernel_spmd

    p = np.arange(P)
    ident = np.eye(P, dtype=np.float32)
    group = np.where(p[:, None] // 8 == p[None, :] // 8, np.float32(1 / 8), np.float32(0)).astype(np.float32)
    chscale = np.stack([np.where(p // n % 2 == 1, 1 / 32, 1.0) for n in (DXA, KW7 - DXA)], 1).astype(np.float32)
    m = np.arange(64)
    icentre = ((p[:, None] // 4 == m[None, :] // 2) & (p[:, None] % 4 == m[None, :] % 2 + 1)).astype(np.float32)

    as_np = np.asarray
    arrays = {
        "x": as_np(x), "mlp_w": as_np(L0_conv_mlp_w), "mlp_b": as_np(L0_conv_mlp_b),
        "conv_wt": np.ascontiguousarray(as_np(L0_conv_conv_w)[:, :, 0, 0].T),
        "conv_b": as_np(L0_conv_conv_b),
        "att_wt": np.ascontiguousarray(as_np(L0_conv_convout_w).transpose(2, 1, 3, 0)).reshape(14, 7, 32),
        "att_b": as_np(L0_conv_convout_b),
        "c3_wt": np.ascontiguousarray(as_np(L1_conv_weight).transpose(2, 3, 1, 0)),
        "c3_b": as_np(L1_conv_bias),
        "ident_c": ident, "group_c": group, "chscale_c": chscale, "icentre_c": icentre,
    }
    nc = bacc.Bacc("TRN2", target_bir_lowering=False, num_devices=1)
    args = [nc.dram_tensor(n + "_dram", a.shape, F32, kind="ExternalInput").ap() for n, a in arrays.items()]
    out = nc.dram_tensor("out_dram", arrays["x"].shape, F32, kind="ExternalOutput").ap()
    build(nc, *args, out)
    r = run_bass_kernel_spmd(nc, [{n + "_dram": a for n, a in arrays.items()}], core_ids=[0])
    return r.results[0]["out_dram"]
```

```python
from contextlib import ExitStack

import concourse.bass as bass
from concourse import mybir

ALU = mybir.AluOpType
ACT = mybir.ActivationFunctionType
F32 = mybir.dt.float32
AX_X = mybir.AxisListType.X

P = 128
EPS = 1e-5
SUB = 4
ROWS = 8
TILES = 512 // ROWS
KW7 = 7
WIN7 = ROWS + KW7 - 1
DXN = 4
XRING = 12
LRING = 3
PEELED = 2

LAG_GATED, LAG_ADD, LAG_Y = 8, 9, 10
LAG_PE, LAG_ACT, LAG_WIN = 10, 12, 12
LAST = 13
AT_X = {"means": 67, "group_mean": 66, "spread": 69, "group_var": 68, "variance": 71, "root": 71,
        "scale": 72, "fold": 71, "bias": 74}
AT_Y = {"means": 1, "group_mean": 0, "spread": 3, "group_var": 2, "variance": 5, "root": 5,
        "scale": 6, "fold": 4, "bias": 8}
EARLY_GATES = 2
Y_ROWS = 11


class Step:

    def __init__(self, turn, place, sums=None):
        self.turn, self.place, self.sums = turn, place, sums

    def number(self):
        return XRING * self.turn + self.place

    def back(self, lag):
        return Step(self.turn, self.place - lag, self.sums)

    def fixed(self):
        return isinstance(self.turn, int)

    def is_at(self, number):
        return self.fixed() and self.number() == number

    def after(self, steps):
        return not self.fixed() or self.number() >= steps

    def exists(self):
        return not self.fixed() or 0 <= self.number() < TILES

    def sum(self, eng, b, per_batch, per_turn, rest):
        if self.fixed():
            return b * per_batch + (per_turn * self.turn + rest)
        key = per_batch, per_turn
        if key not in self.sums:
            self.sums[key] = eng.snap(b * per_batch + self.turn * per_turn)
        return self.sums[key] + rest


def run_steps(eng, body):
    for n in range(PEELED * XRING):
        body(Step(0, n))
    with eng.Fori(PEELED, TILES // XRING) as i:
        sums = {}
        for j in range(XRING):
            body(Step(i, j, sums))
    for n in range(TILES // XRING * XRING, TILES + LAST):
        body(Step(0, n))


def count(eng, b, step, ago=0, batches_ago=0):
    return step.sum(eng, b, TILES, XRING, step.place + 1 - ago - batches_ago * TILES)


def slot_uses(slot, ring):
    return len(range(slot, TILES, ring))


def slot_count(eng, b, step, ring, ago=0, batches_ago=0, dmas=1):
    slot, each = step.place % ring, 16 * dmas
    uses = slot_uses(slot, ring)
    return step.sum(eng, b, each * uses, each * (XRING // ring),
                    each * (step.place // ring + 1 - ago - batches_ago * uses))


def build(nc, x, mlp_w, mlp_b, conv_wt, conv_b, att_wt, att_b, c3_wt, c3_b,
          ident_c, group_c, chscale_c, icentre_c, out):
    B, C, H, W = x.shape
    assert C * SUB == P and 2 * W == 1024
    assert TILES == H // ROWS
    N = 2 * W
    HW2 = W // 2
    CH = W // P
    SROW = W + KW7 + 1
    SH = H + KW7 - 1
    K7 = WIN7 * 2 * DXN
    YH = H + 2
    T3 = ROWS // 2
    W3 = W + 2

    with ExitStack() as ctx:
        def sb(name, shape):
            return ctx.enter_context(nc.sbuf_tensor(name, shape, F32))

        def sem(name):
            return ctx.enter_context(nc.semaphore(name))

        def sems(name, n):
            return [sem(f"{name}{i}") for i in range(n)]


        pooled_d = nc.dram_tensor("pooled_scratch", (SH, 2, SROW), F32, kind="Internal").ap()
        y_d = nc.dram_tensor("y_scratch", (2, C, YH, W), F32, kind="Internal").ap()

        ps = ctx.enter_context(nc.psum_tensor("ps", [P, 8, 512], F32))
        ps_mix = ps[:, 0:2, :]
        ps_tr = ps[:, 2:4, :]
        ps_att = ps[:, 4:6, :]
        ps_parx, ps_pary = ps[:, 0, 0:4], ps[:, 6, 0:4]

        def c3_bank(tiles, chunk, u):
            return ps[:, 6 + u, :] if tiles else ps[:, chunk.place % 2 * 2 + u, :]

        def st_apart(chunks, tile):
            return not chunks or (tile.fixed() and tile.number() < LAG_PE - 2)

        def st_bank(chunks, tile):
            return ps[:, 7 if st_apart(chunks, tile) else 2, 0:P]

        ident = sb("ident", [P, P])
        group = sb("group", [P, P])
        chscale = sb("chscale", [P, 1])
        icentre = sb("icentre", [P, 64])
        mix_w = sb("mix_w", [P, 2, P])
        mix_s = sb("mix_s", [P, 2, P])
        att_wa = sb("att_wa", [K7, 2, P])
        att_wb = sb("att_wb", [K7, 2, P])
        c3_w = sb("c3_w", [P, 3, 64])
        c3_s = sb("c3_s", [P, 3, 64])
        c3_f = sb("c3_f", [P, 64])
        zeros = sb("zeros", [P, SROW])
        wcol = sb("wcol", [P, 1])
        twob = sb("twob", [P, 1])
        mixb = sb("mixb", [P, 1])
        attb = sb("attb", [P, 1])
        c3b = sb("c3b", [P, 1])
        px = sb("px", [P, 16])
        py = sb("py", [P, 16])

        idle = sb("idle", [P, 1])

        xt = sb("xt", [P, XRING, N])
        mixed = sb("mixed", [P, XRING, N])
        win = sb("win", [P, LRING, T3, W3])
        hmax = sb("hmax", [P, 2, HW2])
        hsum = sb("hsum", [P, 2, HW2])
        vsum = sb("vsum", [P, W])
        vmax = sb("vmax", [P, W])
        gate = sb("gate", [P, 2, HW2])
        prod = sb("prod", [P, 2, N])
        stages = prod[:, :, :].rearrange("p a n -> p (a n)")
        stage_mix, stage_a, stage_b = (
            stages[0:k, n * 2 * P:(n + 1) * 2 * P].rearrange("p (a s o) -> p a s o", s=SUB, o=C)
            for n, k in enumerate((P, K7, K7)))
        stage_3 = stages[:, 6 * P:6 * P + 6 * C].rearrange("p (a r o) -> p a r o", r=2, o=C)
        sig = sb("sig", [P, 2, N])
        stat = sb("stat", [P, 2, P])
        statT = sb("statT", [64, 3, P])
        im = sb("im", [K7, 3, W + DXN])
        bnx = sb("bnx", [P, TILES, 2, 6])
        bny = sb("bny", [P, TILES, 2, 6])
        xa = sb("xa", [P, LRING, N])
        ot = sb("ot", [P, LRING, 2, W])
        mrow = sb("mrow", [P, W])

        consts = sem("consts")
        zeros_set = sem("zeros_set")
        stage_zero = sem("stage_zero")
        zeroed = sem("zeroed")
        weights_in = sem("weights_in")
        weights_set = sem("weights_set")
        x0_in = sems("x0_in", XRING)
        xa_in = sems("xa_in", LRING)
        bnx_done = sem("bnx_done")
        small = sems("small", 2)
        agg_ready = sems("agg_ready", 2)
        par_mm = sems("par_mm", 2)
        root_asked = sems("root_asked", 2)
        root_done = sems("root_done", 2)
        x_ready = sem("x_ready")
        y_ready = sem("y_ready")
        pad_rows = sem("pad_rows")
        between = sem("between")
        x_in = sems("x_in", XRING)
        vmax_done = sem("vmax_done")
        hmax_done = sem("hmax_done")
        vsum_done = sem("vsum_done")
        hsum_done = sem("hsum_done")
        garg_done = sem("garg_done")
        gate_done = sem("gate_done")
        prod_done = sem("prod_done")
        mix_done = sem("mix_done")
        mixed_done = sem("mixed_done")
        tr_done = sem("tr_done")
        stat_done = sem("stat_done")
        st_done = sem("st_done")
        statT_done = sem("statT_done")
        pooled_out = sems("pooled_out", 3)
        im_in = sems("im_in", 3)
        att_done = sem("att_done")
        sig_done = sem("sig_done")
        gated = sem("gated")
        y_done = sem("y_done")
        bny_done = sem("bny_done")
        y_out = sems("y_out", XRING)
        win_in = sems("win_in", LRING)
        c3_done = sems("c3_done", 2)
        out_done = sems("out_done", 2)
        chunks_through = sem("chunks_through")
        o_out = sems("o_out", LRING)

        def x_tile_at(b, k):
            return b * (C * H * W) + k * (ROWS * W)

        def x_tile(at):
            return bass.AP(x.tensor, at, [[H * W, C], [N, SUB], [1, N]])

        def y_tile(b, k):
            return bass.AP(y_d.tensor, (b % 2) * (C * YH * W) + k * (ROWS * W) + W, [[YH * W, C], [N, SUB], [1, N]])

        def settled(eng, value):
            return value if isinstance(value, int) else eng.snap(value)

        def taps(at):
            return bass.AP(pooled_d.tensor, at,
                           [[2 * SROW, WIN7], [SROW, 2], [1, DXN], [1, W + DXN]])

        def y_window(at):
            return bass.AP(y_d.tensor, at, [[YH * W, C], [W, 4], [1, W]])

        def out_rows(b, q, g, u):
            return bass.AP(out.tensor, b * (C * H * W) + q * (ROWS * W) + (4 * g + 2 * u) * W,
                           [[H * W, C], [W, 2], [1, W]])

        def pooled_rows(k, a):
            return bass.AP(pooled_d.tensor, k * (ROWS * 2 * SROW) + 3 * (2 * SROW) + a * SROW + 3,
                           [[2 * SROW, ROWS], [1, W]])

        block = ctx.enter_context(nc.Block())

        @block.sync
        def _(sp):
            def load_first(n):
                sp.dma_start(xt[:, n % XRING, :], x_tile(x_tile_at(0, n))).then_inc(x0_in[n % XRING], 16)

            for n in range(XRING):
                load_first(n)

            def load_stat(b, step):
                slot = step.place % LRING
                counted = settled(sp, count(sp, b, step, LRING, -1) if step.after(LRING) else (b + 1) * TILES)
                at = settled(sp, x_tile_at(b + 1, step.number()))
                sp.wait_ge(bnx_done, counted)
                sp.dma_start(xa[:, slot, :], x_tile(at)).then_inc(xa_in[slot], 16)

            def load_taps(b, tile, nxt):
                slot = tile.place % 3
                if nxt.exists():
                    written = settled(sp, slot_count(sp, b, nxt, 3, dmas=2))
                if tile.after(3):
                    used = settled(sp, count(sp, b, tile, 3))
                at = settled(sp, tile.number() * (ROWS * 2 * SROW))
                if nxt.exists():
                    sp.wait_ge(pooled_out[nxt.place % 3], written)
                    sp.sem_inc(between, 1)
                if tile.after(3):
                    sp.wait_ge(att_done, used)
                sp.dma_start(im[:, slot, :], taps(at)).then_inc(im_in[slot], 16)

            def load_x(b, step):
                slot = step.place % XRING
                first = isinstance(b, int) and b == 0 and not step.after(XRING)
                uses = slot_uses(slot, XRING)
                before = slot + (uses - 1) * XRING + 1
                if step.after(XRING):
                    stored = settled(sp, slot_count(sp, b, step, XRING, 1))
                    counted = settled(sp, count(sp, b, step, XRING))
                elif not first:
                    stored = settled(sp, b * (16 * uses))
                    counted = settled(sp, b * TILES - TILES + before)
                at = settled(sp, x_tile_at(b, step.number()))
                if first:
                    sp.wait_ge(bnx_done, before)
                else:
                    sp.wait_ge(y_out[slot], stored)
                    sp.sem_inc(between, 1)
                    sp.wait_ge(bny_done, counted)
                sp.dma_start(xt[:, slot, :], x_tile(at)).then_inc(x_in[slot], 16)

            def pad_y(b):
                stored = [settled(sp, b * (16 * slot_uses(slot, XRING))) for slot in range(XRING)]
                ready = settled(sp, b * 1)
                padded = settled(sp, b * 32)
                place = settled(sp, (b + 1) % 2 * (C * YH * W))
                for slot in range(XRING):
                    sp.wait_ge(y_out[slot], stored[slot])
                    sp.sem_inc(between, 1)
                sp.wait_ge(y_ready, ready)
                for row in (0, YH - 1):
                    sp.dma_start(bass.AP(y_d.tensor, place + row * W, [[YH * W, C], [1, W]]), mrow[::SUB, :])\
                        .then_inc(pad_rows, 16)
                sp.wait_ge(pad_rows, padded)
                sp.sem_inc(between, 1)

            def load_windows(b, chunk):
                slot = chunk.place % LRING
                if chunk.after(LRING):
                    used = settled(sp, count(sp, b, chunk, LRING, batches_ago=1))
                at = [settled(sp, (b + 1) % 2 * (C * YH * W) + chunk.number() * (ROWS * W) + t * (2 * W))
                      for t in range(T3)]
                if chunk.after(LRING):
                    sp.wait_ge(c3_done[1], used)
                for t in range(T3):
                    sp.dma_start(win[:, slot, t, 1:1 + W], y_window(at[t])).then_inc(win_in[slot], 16)

            def stage(b, tiles, chunks, stats):
                def body(step):
                    tile, chunk = step.back(8), step.back(LAG_WIN)
                    if tiles and tile.exists():
                        load_taps(b, tile, step.back(7))
                    if tiles and step.exists():
                        load_x(b, step)
                    if chunks and step.is_at(Y_ROWS):
                        pad_y(b)
                    if chunks and chunk.exists():
                        load_windows(b, chunk)
                    if stats and step.exists():
                        load_stat(b, step)
                run_steps(sp, body)

            for n in range(XRING, TILES):
                sp.wait_ge(bnx_done, n - XRING + 1)
                load_first(n)
            stage(0, True, False, True)
            with sp.Fori(1, B - 1) as b:
                stage(b, True, True, True)
            stage(B - 1, True, True, False)
            stage(B, False, True, False)

        @block.gpsimd
        def _(pool):
            def layer0(b):
                def body(step):
                    if step.exists():
                        slot, two = step.place % XRING, step.place % 2
                        pool.wait_ge(x_in[slot], slot_count(pool, b, step, XRING))
                        pool.tensor_tensor(vsum[:, :], xt[:, slot, 0:W], xt[:, slot, W:N], ALU.add)\
                            .then_inc(vsum_done, 1)
                        pool.wait_ge(vsum_done, count(pool, b, step))
                        if step.after(2):
                            pool.wait_ge(garg_done, count(pool, b, step, 2))
                        v = vsum[:, :].rearrange("p (j t) -> p j t", t=2)
                        pool.tensor_tensor(hsum[:, two, :], v[:, :, 0], v[:, :, 1], ALU.add)\
                            .then_inc(hsum_done, 1)
                        pool.wait_ge(hsum_done, count(pool, b, step))
                    tile = step.back(LAG_GATED)
                    if tile.exists():
                        slot = tile.place % XRING
                        pool.wait_ge(sig_done, count(pool, b, tile))
                        pool.wait_ge(tr_done, count(pool, b, tile))
                        pool.tensor_tensor(mixed[:, slot, :], mixed[:, slot, :], sig[:, tile.place % 2, :],
                                           ALU.mult).then_inc(gated, 1)
                    tile = step.back(LAG_ADD)
                    if tile.exists():
                        slot = tile.place % XRING
                        pool.wait_ge(gated, count(pool, b, tile))
                        pool.tensor_tensor(xt[:, slot, :], xt[:, slot, :], mixed[:, tile.place % XRING, :],
                                           ALU.add).then_inc(y_done, 1)
                run_steps(pool, body)

            with pool.Fori(0, B) as b:
                layer0(b)

        @block.scalar
        def _(act):
            def root(n, turn, par):
                act.wait_ge(root_asked[n], turn + 1)
                act.activation(par[:, 12:13], par[:, 11:12], ACT.Sqrt).then_inc(root_done[n], 1)

            def evacuate(b, tiles, chunk, u):
                slot = chunk.place % LRING
                act.wait_ge(c3_done[u], count(act, b, chunk, batches_ago=1))
                if u == 0:
                    act.wait_ge(o_out[slot], slot_count(act, b, chunk, LRING, 1, dmas=4, batches_ago=1) + 16)
                act.activation(ot[:, slot, u, :], c3_bank(tiles, chunk, u), ACT.Identity, bias=py[:, 9:10])\
                    .then_inc(out_done[u], 1)

            def open_gate(b, step, batches_ago=0):
                two = step.place % 2
                act.wait_ge(garg_done, count(act, b, step, batches_ago=batches_ago))
                if step.after(2):
                    act.wait_ge(prod_done, count(act, b, step, 2))
                act.activation(gate[:, two, :], hmax[:, two, :], ACT.Sigmoid,
                               bias=px[:, 7:8], scale=px[:, 6:7]).then_inc(gate_done, 1)

            def stage(b, tiles, chunks, next_tiles):
                def body(step):
                    tile = step.back(LAG_Y)
                    if tiles and tile.exists():
                        slot = tile.place % XRING
                        act.wait_ge(y_done, count(act, b, tile))
                        act.dma_start(y_tile(b, tile.number()), xt[:, slot, :]).then_inc(y_out[slot], 16)
                    chunk = step.back(LAG_ACT + 1)
                    if chunks and chunk.exists():
                        slot = chunk.place % LRING
                        for u in range(2):
                            act.wait_ge(out_done[u], count(act, b, chunk, batches_ago=1))
                            for g in range(2):
                                act.dma_start(out_rows(b - 1, chunk.number(), g, u),
                                              ot[64 * g:64 * g + 64, slot, u, :]).then_inc(o_out[slot], 16)
                    tile = step.back(2)
                    if tiles and tile.exists():
                        slot = tile.place % XRING
                        act.wait_ge(mix_done, count(act, b, tile))
                        if tile.after(XRING):
                            act.wait_ge(y_done, count(act, b, tile, XRING))
                        act.activation(mixed[:, slot, :], ps_mix.rearrange("p a n -> p (a n)"),
                                       ACT.Identity, bias=px[:, 9:10]).then_inc(mixed_done, 1)
                    if tiles and step.exists() and (not step.fixed() or step.number() >= EARLY_GATES):
                        open_gate(b, step)
                    chunk = step.back(LAG_ACT)
                    if chunks and chunk.exists():
                        evacuate(b, tiles, chunk, 0)
                    tile = step.back(7)
                    if tiles and tile.exists():
                        act.wait_ge(att_done, count(act, b, tile))
                        if tile.after(2):
                            act.wait_ge(gated, count(act, b, tile, 2))
                        act.activation(sig[:, tile.place % 2, :], ps_att.rearrange("p a n -> p (a n)"),
                                       ACT.Sigmoid, bias=attb[:, :]).then_inc(sig_done, 1)
                    tile = step.back(4)
                    if tiles and tile.exists():
                        slot = tile.place % 3
                        act.wait_ge(st_done, count(act, b, tile))
                        if tile.after(3):
                            act.wait_ge(pooled_out[slot], slot_count(act, b, tile, 3, 1, dmas=2))
                        act.activation(statT[:, slot, :], st_bank(chunks, tile)[0:64, :], ACT.Copy)\
                            .then_inc(statT_done, 1)
                        act.wait_ge(statT_done, count(act, b, tile))
                        for a in range(2):
                            act.dma_start(pooled_rows(tile.number(), a), statT[32 * a:32 * a + 32, slot, :])\
                                .then_inc(pooled_out[slot], 16)
                    if chunks and chunk.exists():
                        evacuate(b, tiles, chunk, 1)
                    if chunks and step.is_at(AT_Y["root"]):
                        root(1, b - 1, py)
                    if next_tiles and step.is_at(AT_X["root"]):
                        root(0, b + 1, px)
                    for n in range(EARLY_GATES):
                        if next_tiles and step.is_at(AT_X["bias"] + n):
                            if n == 0:
                                act.wait_ge(x_ready, b + 2)
                            open_gate(b, Step(0, n), batches_ago=-1)
                run_steps(act, body)
                act.sem_inc(chunks_through, 1)

            small_loads = [
                (ident[:, :], ident_c), (group[:, :], group_c), (chscale[:, :], chscale_c),
                (icentre[:, :], icentre_c),
                (wcol[:, :], bass.AP(mlp_w.tensor, 0, [[0, P], [1, 1]])),
                (twob[:, :], bass.AP(mlp_b.tensor, 0, [[0, P], [1, 1]])),
                (mixb[:, :], bass.AP(conv_b.tensor, 0, [[1, C], [0, SUB], [1, 1]])),
                (attb[:, :], bass.AP(att_b.tensor, 0, [[1, C], [0, SUB], [1, 1]])),
                (c3b[0:64, :], bass.AP(c3_b.tensor, 0, [[1, C], [0, 2], [1, 1]])),
                (c3b[64:P, :], bass.AP(c3_b.tensor, 0, [[1, C], [0, 2], [1, 1]])),
            ]
            for dst, src in small_loads:
                act.dma_start(dst, src).then_inc(consts, 16)
            act.wait_ge(stage_zero, 1)
            n = 0
            for s in range(SUB):
                for part in range(2):
                    act.dma_start(stage_mix[s::SUB, part, s, :], conv_wt[part * C:(part + 1) * C, :])\
                        .then_inc(weights_in, 16)
                    n += 1
                for r in range(2):
                    row = 2 * s + r
                    for taps_stage, dx0 in ((stage_a, 0), (stage_b, DXN)):
                        act.dma_start(taps_stage[row * 2 * DXN:(row + KW7) * 2 * DXN, r, s, :],
                                     att_wt[:, dx0:dx0 + DXN, :]).then_inc(weights_in, 16)
                        n += 1
            for r in range(2):
                for dy in range(3):
                    act.dma_start(stage_3[r + dy::4, :, r, :], c3_wt[dy].rearrange("d c o -> c d o"))\
                        .then_inc(weights_in, 16)
                    n += 1
            assert n == WEIGHT_LOADS
            act.wait_ge(zeros_set, 2)
            rows = pooled_d.rearrange("h c w -> (h c) w")
            for at in range(0, 2 * SH, P):
                m = min(P, 2 * SH - at)
                act.dma_start(rows[at:at + m, :], zeros[0:m, :]).then_inc(zeroed, 16)
            act.wait_ge(zeroed, 16 * -(-2 * SH // P))
            for slot in range(LRING):
                act.sem_inc(o_out[slot], 16)
            act.wait_ge(consts, 16 * 10)
            root(0, 0, px)
            act.wait_ge(x_ready, 1)
            for n in range(EARLY_GATES):
                open_gate(0, Step(0, n))
            stage(0, True, False, True)
            with act.Fori(1, B - 1) as b:
                stage(b, True, True, True)
            stage(B - 1, True, True, False)
            stage(B, False, True, False)
            for slot in range(LRING):
                act.wait_ge(o_out[slot], B * (64 * slot_uses(slot, LRING)) + 16)

        @block.tensor
        def _(pe):
            def group_mean(n, turn, par, ps_par):
                pe.wait_ge(agg_ready[n], 3 * turn + 1)
                pe.matmul(ps_par[:, 0:1], group[:, :], par[:, 0:1], start=True, stop=True)\
                    .then_inc(par_mm[n], 1)

            def group_var(n, turn, par, ps_par):
                pe.wait_ge(agg_ready[n], 3 * turn + 2)
                pe.matmul(ps_par[:, 1:2], group[:, :], par[:, 3:4], start=True, stop=True)\
                    .then_inc(par_mm[n], 1)

            def fold_x(turn):
                pe.wait_ge(agg_ready[0], 3 * turn + 3)
                pe.matmul(ps_parx[:, 2:3], mix_s[:, 1, :], px[:, 4:5], start=True, stop=True)\
                    .then_inc(par_mm[0], 1)

            def fold_y(turn):
                pe.wait_ge(agg_ready[1], 3 * turn + 3)
                for g in range(2):
                    for dx in range(3):
                        last = pe.matmul(ps_pary[64 * g:64 * g + 64, 2:3], c3_s[:, dx, :], py[:, 4:5],
                                         start=(dx == 0), stop=(dx == 2))
                last.then_inc(par_mm[1], 1)

            def convolve(b, tiles, chunk, u):
                slot = chunk.place % LRING
                if u == 0:
                    pe.wait_ge(win_in[slot], slot_count(pe, b, chunk, LRING, dmas=T3, batches_ago=1))
                if not tiles:
                    if chunk.after(2):
                        pe.wait_ge(out_done[u], count(pe, b, chunk, 2, batches_ago=1))
                elif chunk.after(1):
                    pe.wait_ge(out_done[u], count(pe, b, chunk, 1, batches_ago=1))
                bank = c3_bank(tiles, chunk, u)
                for n, dx in enumerate((1, 0, 2)):
                    w = c3_f[:, :] if dx == 1 else c3_s[:, dx, :]
                    for g in range(2):
                        last = pe.matmul(bank[64 * g:64 * g + 64, :], w, win[:, slot, 2 * g + u, dx:dx + W],
                                         start=(n == 0), stop=(n == 2))
                last.then_inc(c3_done[u], 1)

            def stage(b, tiles, chunks, next_tiles):
                if tiles:
                    pe.wait_ge(x_ready, b + 1)

                def body(step):
                    if chunks and step.is_at(LAG_PE):
                        pe.wait_ge(y_ready, b)
                    if tiles and step.exists():
                        slot, two = step.place % XRING, step.place % 2
                        pe.wait_ge(x_in[slot], slot_count(pe, b, step, XRING))
                        if step.after(1):
                            pe.wait_ge(mixed_done, count(pe, b, step, 1))
                        for r in range(2):
                            pe.matmul(ps_mix[:, r, :], mix_s[:, 1, :], xt[:, slot, r * W:(r + 1) * W],
                                      start=True, stop=False)
                        pe.wait_ge(prod_done, count(pe, b, step))
                        for r in range(2):
                            last = pe.matmul(ps_mix[:, r, :], mix_s[:, 0, :], prod[:, two, r * W:(r + 1) * W],
                                             start=False, stop=True)
                        last.then_inc(mix_done, 1)
                    chunk = step.back(LAG_PE)
                    if chunks and chunk.exists():
                        convolve(b, tiles, chunk, 0)
                    tile = step.back(5)
                    if tiles and tile.exists():
                        slot = tile.place % 3
                        pe.wait_ge(im_in[slot], slot_count(pe, b, tile, 3))
                        if tile.after(1):
                            pe.wait_ge(sig_done, count(pe, b, tile, 1))
                        for r in range(2):
                            pe.matmul(ps_att[:, r, :], att_wa[:, r, :], im[:, slot, 0:W], start=True, stop=False)
                            last = pe.matmul(ps_att[:, r, :], att_wb[:, r, :], im[:, slot, DXN:DXN + W],
                                             start=False, stop=True)
                        last.then_inc(att_done, 1)
                    turned = step.back(2)
                    if tiles and turned.exists():
                        if st_apart(chunks, turned):
                            pe.wait_ge(stat_done, count(pe, b, turned))
                        else:
                            last_tile = step.back(1)
                            pe.wait_ge(stat_done, count(pe, b, last_tile if last_tile.exists() else turned))
                        if turned.after(1):
                            pe.wait_ge(statT_done, count(pe, b, turned, 1))
                        pe.transpose(st_bank(chunks, turned), stat[:, turned.place % 2, :], ident[:, :])\
                            .then_inc(st_done, 1)
                    if chunks and chunk.exists():
                        convolve(b, tiles, chunk, 1)
                    if tiles and step.exists():
                        slot = step.place % XRING
                        pe.wait_ge(mixed_done, count(pe, b, step))
                        if step.after(1):
                            pe.wait_ge(stat_done, count(pe, b, step, 1))
                        if turned.exists() and not st_apart(chunks, turned):
                            pe.wait_ge(statT_done, count(pe, b, turned))
                        for n in range(2 * CH):
                            last = pe.transpose(ps_tr[:, n // CH, n % CH * P:n % CH * P + P],
                                                mixed[:, slot, n * P:(n + 1) * P], ident[:, :])
                        last.then_inc(tr_done, 1)
                    if chunks:
                        if step.is_at(AT_Y["group_mean"]):
                            group_mean(1, b - 1, py, ps_pary)
                        if step.is_at(AT_Y["group_var"]):
                            group_var(1, b - 1, py, ps_pary)
                        if step.is_at(AT_Y["fold"]):
                            fold_y(b - 1)
                    if next_tiles:
                        if step.is_at(AT_X["group_mean"]):
                            group_mean(0, b + 1, px, ps_parx)
                        if step.is_at(AT_X["group_var"]):
                            group_var(0, b + 1, px, ps_parx)
                        if step.is_at(AT_X["fold"]):
                            fold_x(b + 1)
                run_steps(pe, body)

            pe.wait_ge(consts, 16 * 10)
            pe.wait_ge(weights_set, 5)
            group_mean(0, 0, px, ps_parx)
            group_var(0, 0, px, ps_parx)
            fold_x(0)
            stage(0, True, False, True)
            with pe.Fori(1, B - 1) as b:
                stage(b, True, True, True)
            stage(B - 1, True, True, False)
            stage(B, False, True, False)

        @block.vector
        def _(dve):
            SMALL_X, SMALL_Y = 12, 9

            dve.memset(stages, 0.0).then_inc(stage_zero, 1)
            dve.memset(zeros[:, :], 0.0).then_inc(zeros_set, 1)
            dve.memset(stat[:, :, :], 0.0).then_inc(zeros_set, 1)
            def count_x(b, step):
                slot = step.place % LRING
                dve.wait_ge(xa_in[slot], slot_count(dve, b, step, LRING))
                for r in range(2):
                    last = dve.bn_stats(bnx_at(step, r), xa[:, slot, r * W:(r + 1) * W])
                last.then_inc(bnx_done, 1)

            def bnx_at(step, r):
                return bnx[:, bass.ds(step.number(), 1), r, :].rearrange("p a n -> p (a n)")

            def bny_at(step, r):
                return bny[:, bass.ds(step.number(), 1), r, :].rearrange("p a n -> p (a n)")

            class Chain:

                def __init__(self, n, base):
                    self.done, self.base, self.at = small[n], base, 0

                def __call__(self, ins, follows=True):
                    self.at += 1
                    ins.then_inc(self.done, 1)
                    if follows:
                        dve.wait_ge(self.done, self.base + self.at)

            def means(n, chain, par, stats):
                dve.memset(idle[:, :], 0.0)
                chain(dve.bn_aggr(par[:, 0:2], stats[:, :, :, :].rearrange("p a b c -> p (a b c)")))
                dve.sem_inc(agg_ready[n], 1)

            def spread(n, turn, chain, par, ps_par):
                dve.wait_ge(par_mm[n], 3 * turn + 1)
                chain(dve.tensor_scalar(par[:, 2:3], par[:, 0:1], ps_par[:, 0:1], None, ALU.subtract))
                chain(dve.tensor_copy(par[:, 4:5], ps_par[:, 0:1]), follows=False)
                dve.scalar_tensor_tensor(out=par[:, 3:4], in0=par[:, 2:3], scalar=par[:, 2:3], in1=par[:, 1:2],
                                         op0=ALU.mult, op1=ALU.add).then_inc(agg_ready[n], 1)

            def variance(n, turn, chain, par, ps_par):
                dve.wait_ge(par_mm[n], 3 * turn + 2)
                chain(dve.tensor_scalar(par[:, 11:12], ps_par[:, 1:2], EPS, None, ALU.add))
                dve.sem_inc(root_asked[n], 1)

            def scale(n, turn, chain, par):
                dve.wait_ge(root_done[n], turn + 1)
                chain(dve.reciprocal(par[:, 13:14], par[:, 12:13]))
                chain(dve.tensor_scalar(par[:, 14:15], par[:, 13:14], par[:, 13:14], par[:, 11:12],
                                        ALU.mult, ALU.mult))
                chain(dve.tensor_scalar(par[:, 15:16], par[:, 14:15], -0.5, 1.5, ALU.mult, ALU.add))
                chain(dve.tensor_scalar(par[:, 5:6], par[:, 15:16], par[:, 13:14], None, ALU.mult))

            def scale_x(turn, chain):
                scale(0, turn, chain, px)
                chain(dve.tensor_scalar(px[:, 6:7], px[:, 5:6], wcol[:, 0:1], None, ALU.mult))
                chain(dve.tensor_scalar(px[:, 8:9], px[:, 4:5], -1.0, None, ALU.mult))
                chain(dve.tensor_scalar(px[:, 10:11], px[:, 8:9], px[:, 6:7], 2.0, ALU.mult, ALU.mult))
                chain(dve.tensor_scalar(px[:, 7:8], px[:, 10:11], twob[:, 0:1], None, ALU.add))
                dve.tensor_scalar(mix_s[:, :, :], mix_w[:, :, :], px[:, 5:6], None, ALU.mult)\
                    .then_inc(agg_ready[0], 1)

            def bias_x(turn, chain):
                dve.wait_ge(par_mm[0], 3 * turn + 3)
                dve.scalar_tensor_tensor(out=px[:, 9:10], in0=ps_parx[:, 2:3], scalar=-1.0, in1=mixb[:, :],
                                         op0=ALU.mult, op1=ALU.add).then_inc(x_ready, 1)
                assert chain.at == SMALL_X

            def scale_y(turn, chain):
                scale(1, turn, chain, py)
                dve.tensor_scalar(c3_s[:, :, :], c3_w[:, :, :], py[:, 5:6], None, ALU.mult)\
                    .then_inc(agg_ready[1], 1)
                dve.wait_ge(agg_ready[1], 3 * turn + 3)
                dve.tensor_tensor(c3_f[:, :], c3_s[:, 1, :], icentre[:, :], ALU.add)
                dve.tensor_scalar(mrow[:, :], zeros[:, 0:W], py[:, 4:5], None, ALU.add)
                for slot in range(LRING):
                    dve.tensor_scalar(win[:, slot, :, 0:W3:W3 - 1],
                                      zeros[:, 0:2 * T3].rearrange("p (a b) -> p a b", b=2),
                                      py[:, 4:5], None, ALU.add)

            def bias_y(turn, chain):
                dve.wait_ge(par_mm[1], 3 * turn + 3)
                chain(dve.scalar_tensor_tensor(out=py[:, 9:10], in0=ps_pary[:, 2:3], scalar=-1.0, in1=c3b[:, :],
                                               op0=ALU.mult, op1=ALU.add))
                dve.sem_inc(y_ready, 1)
                assert chain.at == SMALL_Y

            def means_x(turn, chain):
                dve.wait_ge(bnx_done, (turn + 1) * TILES)
                means(0, chain, px, bnx)

            def means_y(turn, chain):
                dve.wait_ge(bny_done, (turn + 1) * TILES)
                dve.sem_inc(between, 1)
                dve.wait_ge(chunks_through, turn + 1)
                means(1, chain, py, bny)

            def stage(b, tiles, chunks, stats):
                if tiles:
                    dve.wait_ge(x_ready, b + 1)
                chain_x = Chain(0, (b + 1) * SMALL_X)
                chain_y = Chain(1, (b - 1) * SMALL_Y)

                def body(step):
                    if tiles:
                        work_on_tiles(step)
                    if stats and step.exists():
                        count_x(b, step)
                    if chunks:
                        if step.is_at(AT_Y["means"]):
                            means_y(b - 1, chain_y)
                        if step.is_at(AT_Y["spread"]):
                            spread(1, b - 1, chain_y, py, ps_pary)
                        if step.is_at(AT_Y["variance"]):
                            variance(1, b - 1, chain_y, py, ps_pary)
                        if step.is_at(AT_Y["scale"]):
                            scale_y(b - 1, chain_y)
                        if step.is_at(AT_Y["bias"]):
                            bias_y(b - 1, chain_y)
                    if stats:
                        if step.is_at(AT_X["means"]):
                            means_x(b + 1, chain_x)
                        if step.is_at(AT_X["spread"]):
                            spread(0, b + 1, chain_x, px, ps_parx)
                        if step.is_at(AT_X["variance"]):
                            variance(0, b + 1, chain_x, px, ps_parx)
                        if step.is_at(AT_X["scale"]):
                            scale_x(b + 1, chain_x)
                        if step.is_at(AT_X["bias"]):
                            bias_x(b + 1, chain_x)

                def work_on_tiles(step):
                    tile = step.back(3)
                    if tile.exists():
                        two = tile.place % 2
                        dve.wait_ge(tr_done, count(dve, b, tile))
                        if tile.after(2):
                            dve.wait_ge(st_done, count(dve, b, tile, 2))
                        src = ps_tr.rearrange("p a (n c s) -> p s (a n) c", c=C, s=SUB)
                        dst = stat[:, two, 0:64].rearrange("p (t s n) -> p t s n", s=SUB, t=2)
                        dve.tensor_reduce(dst[:, 0], src, AX_X, ALU.max)
                        dve.tensor_reduce(dst[:, 1], src, AX_X, ALU.add).then_inc(stat_done, 1)
                    if step.exists():
                        slot = step.place % XRING
                        dve.wait_ge(x_in[slot], slot_count(dve, b, step, XRING))
                        if step.after(1):
                            dve.wait_ge(hmax_done, count(dve, b, step, 1))
                        dve.tensor_tensor(vmax[:, :], xt[:, slot, 0:W], xt[:, slot, W:N], ALU.max)\
                            .then_inc(vmax_done, 1)
                    if step.exists():
                        two = step.place % 2
                        dve.wait_ge(vmax_done, count(dve, b, step))
                        if step.after(2):
                            dve.wait_ge(gate_done, count(dve, b, step, 2))
                        v = vmax[:, :].rearrange("p (j t) -> p j t", t=2)
                        dve.tensor_tensor(hmax[:, two, :], v[:, :, 0], v[:, :, 1], ALU.max)\
                            .then_inc(hmax_done, 1)
                    tile = step.back(1)
                    if tile.exists():
                        slot, two = tile.place % XRING, tile.place % 2
                        dve.wait_ge(gate_done, count(dve, b, tile))
                        if tile.after(2):
                            dve.wait_ge(mix_done, count(dve, b, tile, 2))
                        wide = gate[:, two, :].rearrange("p (j t) -> p j t", t=1).broadcast_to([P, HW2, 2])
                        for r in range(2):
                            row = slice(r * W, (r + 1) * W)
                            last = dve.scalar_tensor_tensor(
                                out=prod[:, two, row].rearrange("p (j t) -> p j t", t=2),
                                in0=xt[:, slot, row].rearrange("p (j t) -> p j t", t=2),
                                scalar=px[:, 8:9], in1=wide, op0=ALU.add, op1=ALU.mult)
                        last.then_inc(prod_done, 1)
                    if step.exists():
                        two = step.place % 2
                        dve.wait_ge(hsum_done, count(dve, b, step))
                        dve.wait_ge(hmax_done, count(dve, b, step))
                        dve.scalar_tensor_tensor(out=hmax[:, two, :], in0=hsum[:, two, :], scalar=0.25,
                                                 in1=hmax[:, two, :], op0=ALU.mult, op1=ALU.add)\
                            .then_inc(garg_done, 1)
                    tile = step.back(LAG_Y)
                    if tile.exists():
                        slot = tile.place % XRING
                        dve.wait_ge(y_done, count(dve, b, tile))
                        for r in range(2):
                            last = dve.bn_stats(bny_at(tile, r), xt[:, slot, r * W:(r + 1) * W])
                        last.then_inc(bny_done, 1)
                run_steps(dve, body)

            def set_weights():
                dve.wait_ge(consts, 16 * 10)
                dve.wait_ge(weights_in, 16 * WEIGHT_LOADS)
                dve.tensor_copy(mix_w[:, :, :].rearrange("p a (o s) -> p a s o", s=SUB), stage_mix[:, :, :, :])\
                    .then_inc(weights_set, 1)
                for taps_stage, dst in ((stage_a, att_wa), (stage_b, att_wb)):
                    dve.tensor_scalar(dst[:, :, :].rearrange("p a (o s) -> p a s o", s=SUB), taps_stage[:, :, :, :],
                                      chscale[0:K7, 0:1], None, ALU.mult).then_inc(weights_set, 1)
                dve.tensor_copy(c3_w[:, :, :].rearrange("p a (o r) -> p a r o", r=2), stage_3[:, :, :, :])\
                    .then_inc(weights_set, 1)
                dve.tensor_scalar(mrow[:, 0:1], twob[:, :], 2.0, None, ALU.mult).then_inc(weights_set, 1)
                dve.wait_ge(weights_set, 5)
                dve.tensor_copy(twob[:, :], mrow[:, 0:1]).then_inc(weights_set, 1)
                dve.wait_ge(weights_set, 6)

            for n in range(TILES):
                if n == TILES - XRING:
                    set_weights()
                dve.wait_ge(x0_in[n % XRING], 16 * (n // XRING + 1))
                for r in range(2):
                    last = dve.bn_stats(bnx[:, n, r, :], xt[:, n % XRING, r * W:(r + 1) * W])
                last.then_inc(bnx_done, 1)
            chain = Chain(0, 0)
            means_x(0, chain)
            spread(0, 0, chain, px, ps_parx)
            variance(0, 0, chain, px, ps_parx)
            scale_x(0, chain)
            bias_x(0, chain)
            stage(0, True, False, True)
            with dve.Fori(1, B - 1) as b:
                stage(b, True, True, True)
            stage(B - 1, True, True, False)
            stage(B, False, True, False)


WEIGHT_LOADS = SUB * (2 + 4) + 6


def kernel(x, L0_conv_mlp_w, L0_conv_mlp_b, L0_conv_conv_w, L0_conv_conv_b, L0_conv_convout_w,
           L0_conv_convout_b, L1_conv_weight, L1_conv_bias):
    import numpy as np
    import concourse.bacc as bacc
    from concourse.bass_utils import run_bass_kernel_spmd

    p = np.arange(P)
    ident = np.eye(P, dtype=np.float32)
    group = np.where(p[:, None] // 8 == p[None, :] // 8, np.float32(1 / 8), np.float32(0)).astype(np.float32)
    chscale = np.where(p // DXN % 2 == 1, 1 / 32, 1.0).astype(np.float32)[:, None]
    m = np.arange(64)
    icentre = ((p[:, None] // 4 == m[None, :] // 2) & (p[:, None] % 4 == m[None, :] % 2 + 1)).astype(np.float32)

    as_np = np.asarray
    arrays = {
        "x": as_np(x), "mlp_w": as_np(L0_conv_mlp_w), "mlp_b": as_np(L0_conv_mlp_b),
        "conv_wt": np.ascontiguousarray(as_np(L0_conv_conv_w)[:, :, 0, 0].T),
        "conv_b": as_np(L0_conv_conv_b),
        "att_wt": np.pad(np.ascontiguousarray(as_np(L0_conv_convout_w).transpose(2, 1, 3, 0)).reshape(14, 7, 32),
                         ((0, 0), (0, 1), (0, 0))),
        "att_b": as_np(L0_conv_convout_b),
        "c3_wt": np.ascontiguousarray(as_np(L1_conv_weight).transpose(2, 3, 1, 0)),
        "c3_b": as_np(L1_conv_bias),
        "ident_c": ident, "group_c": group, "chscale_c": chscale, "icentre_c": icentre,
    }
    nc = bacc.Bacc("TRN2", target_bir_lowering=False, num_devices=1)
    args = [nc.dram_tensor(n + "_dram", a.shape, F32, kind="ExternalInput").ap() for n, a in arrays.items()]
    out = nc.dram_tensor("out_dram", arrays["x"].shape, F32, kind="ExternalOutput").ap()
    build(nc, *args, out)
    r = run_bass_kernel_spmd(nc, [{n + "_dram": a for n, a in arrays.items()}], core_ids=[0])
    return r.results[0]["out_dram"]
```
